# Optimizing a Trainium2 kernel written in Bass

```python
import numpy as np
import jax
import jax.numpy as jnp

def _softmax(x, axis=-1):
    return jax.nn.softmax(x, axis=axis)

def _gelu(x):
    return jax.nn.gelu(x, approximate=True)

def _silu(x):
    return jax.nn.silu(x)

def _sigmoid(x):
    return jax.nn.sigmoid(x)

def _layernorm(x, axis=-1, eps=1e-05):
    m = jnp.mean(x, axis=axis, keepdims=True)
    v = jnp.var(x, axis=axis, keepdims=True)
    return (x - m) / jnp.sqrt(v + eps)

def _scatter_add(tgt, idx, src, axis=0):
    return tgt.at[idx].add(src)

def _segment_sum(src, seg, n):
    return jax.ops.segment_sum(src, seg, n)
kernel_name = 'mk_rec_standalone_d1_rec_r8_900268'

def setup_inputs(seed: int=0):
    np.random.seed(seed)
    _w = jnp.asarray

    def _rec_inputs():
        import jax
        import jax.numpy as jnp
        _rk = jax.random.key(seed)
        r_price = 0.00386106 + 1.00199 * jax.random.normal(jax.random.fold_in(_rk, 1), (2048,), jnp.float32)
        r_x_cat = jnp.stack([jax.random.randint(jax.random.fold_in(jax.random.fold_in(_rk, 2), 0), (2048,), 17, 99964, jnp.int32), jax.random.randint(jax.random.fold_in(jax.random.fold_in(_rk, 2), 1), (2048,), 3, 99987, jnp.int32), jax.random.randint(jax.random.fold_in(jax.random.fold_in(_rk, 2), 2), (2048,), 1, 99978, jnp.int32), jax.random.randint(jax.random.fold_in(jax.random.fold_in(_rk, 2), 3), (2048,), 11, 99990, jnp.int32), jax.random.randint(jax.random.fold_in(jax.random.fold_in(_rk, 2), 4), (2048,), 10, 99996, jnp.int32), jax.random.randint(jax.random.fold_in(jax.random.fold_in(_rk, 2), 5), (2048,), 7, 99998, jnp.int32), jax.random.randint(jax.random.fold_in(jax.random.fold_in(_rk, 2), 6), (2048,), 5, 99990, jnp.int32), jax.random.randint(jax.random.fold_in(jax.random.fold_in(_rk, 2), 7), (2048,), 4, 99996, jnp.int32), jax.random.randint(jax.random.fold_in(jax.random.fold_in(_rk, 2), 8), (2048,), 6, 99995, jnp.int32), jax.random.randint(jax.random.fold_in(jax.random.fold_in(_rk, 2), 9), (2048,), 2, 99998, jnp.int32), jax.random.randint(jax.random.fold_in(jax.random.fold_in(_rk, 2), 10), (2048,), 0, 99993, jnp.int32), jax.random.randint(jax.random.fold_in(jax.random.fold_in(_rk, 2), 11), (2048,), 1, 12500, jnp.int32), jax.random.randint(jax.random.fold_in(jax.random.fold_in(_rk, 2), 12), (2048,), 18, 12500, jnp.int32), jax.random.randint(jax.random.fold_in(jax.random.fold_in(_rk, 2), 13), (2048,), 1, 99995, jnp.int32), jax.random.randint(jax.random.fold_in(jax.random.fold_in(_rk, 2), 14), (2048,), 0, 99998, jnp.int32), jax.random.randint(jax.random.fold_in(jax.random.fold_in(_rk, 2), 15), (2048,), 4, 99999, jnp.int32), jax.random.randint(jax.random.fold_in(jax.random.fold_in(_rk, 2), 16), (2048,), 6, 12498, jnp.int32), jax.random.randint(jax.random.fold_in(jax.random.fold_in(_rk, 2), 17), (2048,), 0, 99997, jnp.int32), jax.random.randint(jax.random.fold_in(jax.random.fold_in(_rk, 2), 18), (2048,), 16, 99994, jnp.int32), jax.random.randint(jax.random.fold_in(jax.random.fold_in(_rk, 2), 19), (2048,), 9, 99997, jnp.int32), jax.random.randint(jax.random.fold_in(jax.random.fold_in(_rk, 2), 20), (2048,), 0, 99981, jnp.int32), jax.random.randint(jax.random.fold_in(jax.random.fold_in(_rk, 2), 21), (2048,), 8, 99999, jnp.int32), jax.random.randint(jax.random.fold_in(jax.random.fold_in(_rk, 2), 22), (2048,), 0, 99988, jnp.int32), jax.random.randint(jax.random.fold_in(jax.random.fold_in(_rk, 2), 23), (2048,), 0, 99993, jnp.int32), jax.random.randint(jax.random.fold_in(jax.random.fold_in(_rk, 2), 24), (2048,), 2, 12499, jnp.int32), jax.random.randint(jax.random.fold_in(jax.random.fold_in(_rk, 2), 25), (2048,), 5, 99988, jnp.int32)], axis=0)
        return (r_price, r_x_cat)
    r_price, r_x_cat = _rec_inputs()

    def _L0_rec_setup():
        import jax, jax.numpy as jnp
        import numpy as np
        NUM_FIELDS = 26
        VOCAB = 12500
        B = 2048
        D = 64
        BM1, BM2 = (128, 64)
        TM1, TM2 = (256, 1)
        NUM_FEATS = NUM_FIELDS + 1
        NUM_INTER = NUM_FEATS * (NUM_FEATS - 1) // 2
        TOP_IN = NUM_INTER + BM2
        _IU, _JU = np.triu_indices(NUM_FEATS, k=1)
        key = jax.random.key(seed)
        ks = jax.random.split(key, 13)
        x_cat = jax.random.randint(ks[0], (NUM_FIELDS, B), 0, VOCAB)
        price = jax.random.normal(ks[1], (B,), dtype=jnp.float32)
        emb_tables = jax.random.normal(ks[2], (NUM_FIELDS, VOCAB, D), dtype=jnp.float32) * 0.05
        Wp = jax.random.normal(ks[3], (1, D), dtype=jnp.float32) * 0.1
        bp = jnp.zeros((D,), jnp.float32)
        W1 = jax.random.normal(ks[4], (D, BM1), dtype=jnp.float32) * 0.1
        b1 = jnp.zeros((BM1,), jnp.float32)
        W2 = jax.random.normal(ks[5], (BM1, BM2), dtype=jnp.float32) * 0.1
        b2 = jnp.zeros((BM2,), jnp.float32)
        Wt1 = jax.random.normal(ks[6], (TOP_IN, TM1), dtype=jnp.float32) * 0.05
        bt1 = jnp.zeros((TM1,), jnp.float32)
        Wt2 = jax.random.normal(ks[7], (TM1, TM2), dtype=jnp.float32) * 0.05
        bt2 = jnp.zeros((TM2,), jnp.float32)
        return {'x_cat': x_cat, 'price': price, 'emb_tables': emb_tables, 'Wp': Wp, 'bp': bp, 'W1': W1, 'b1': b1, 'W2': W2, 'b2': b2, 'Wt1': Wt1, 'bt1': bt1, 'Wt2': Wt2, 'bt2': bt2}
    _L0_rec_all = _L0_rec_setup()
    _L0_rec_in = {k: v for k, v in _L0_rec_all.items() if k in ('emb_tables', 'Wp', 'bp', 'W1', 'b1', 'W2', 'b2', 'Wt1', 'bt1', 'Wt2', 'bt2')}
    del _L0_rec_all
    return {'r_price': r_price, 'r_x_cat': r_x_cat, 'L0_rec_emb_tables': _L0_rec_in['emb_tables'], 'L0_rec_Wp': _L0_rec_in['Wp'], 'L0_rec_bp': _L0_rec_in['bp'], 'L0_rec_W1': _L0_rec_in['W1'], 'L0_rec_b1': _L0_rec_in['b1'], 'L0_rec_W2': _L0_rec_in['W2'], 'L0_rec_b2': _L0_rec_in['b2'], 'L0_rec_Wt1': _L0_rec_in['Wt1'], 'L0_rec_bt1': _L0_rec_in['bt1'], 'L0_rec_Wt2': _L0_rec_in['Wt2'], 'L0_rec_bt2': _L0_rec_in['bt2']}

def reference(r_price, r_x_cat, L0_rec_emb_tables, L0_rec_Wp, L0_rec_bp, L0_rec_W1, L0_rec_b1, L0_rec_W2, L0_rec_b2, L0_rec_Wt1, L0_rec_bt1, L0_rec_Wt2, L0_rec_bt2):
    import jax
    import jax.numpy as jnp

    def _L0_rec_ref(x_cat, price, emb_tables, Wp, bp, W1, b1, W2, b2, Wt1, bt1, Wt2, bt2):
        import jax, jax.numpy as jnp
        import numpy as np
        NUM_FIELDS = 26
        VOCAB = 12500
        B = 2048
        D = 64
        BM1, BM2 = (128, 64)
        TM1, TM2 = (256, 1)
        NUM_FEATS = NUM_FIELDS + 1
        NUM_INTER = NUM_FEATS * (NUM_FEATS - 1) // 2
        TOP_IN = NUM_INTER + BM2
        _IU, _JU = np.triu_indices(NUM_FEATS, k=1)
        emb = emb_tables[jnp.arange(NUM_FIELDS)[:, None], x_cat]
        emb = jnp.transpose(emb, (1, 0, 2))
        dense_embed = price[:, None] @ Wp + bp
        feats = jnp.concatenate([emb, dense_embed[:, None, :]], axis=1)
        gram = jnp.einsum('bid,bjd->bij', feats, feats)
        interactions = gram[:, _IU, _JU]
        h = jax.nn.relu(dense_embed @ W1 + b1)
        dense_out = jax.nn.relu(h @ W2 + b2)
        concat = jnp.concatenate([interactions, dense_out], axis=1)
        t = jax.nn.relu(concat @ Wt1 + bt1)
        out = (t @ Wt2 + bt2)[:, 0]
        return out
    y = _L0_rec_ref(r_x_cat, r_price, L0_rec_emb_tables, L0_rec_Wp, L0_rec_bp, L0_rec_W1, L0_rec_b1, L0_rec_W2, L0_rec_b2, L0_rec_Wt1, L0_rec_bt1, L0_rec_Wt2, L0_rec_bt2)
    return y

_drawn_inputs = setup_inputs


def setup_inputs(seed=0):
    import zlib

    import numpy as np

    out = dict(_drawn_inputs(seed))
    spreads = {'L0_rec_bp': (0.0, 0.1),
     'L0_rec_b1': (0.0, 0.1),
     'L0_rec_b2': (0.0, 0.1),
     'L0_rec_bt1': (0.0, 0.1)}
    factors = {}
    for name, (base, spread) in spreads.items():
        noise = np.random.default_rng([zlib.crc32(name.encode()), seed]).standard_normal(out[name].shape)
        drawn = base * np.exp(spread * noise) if base else spread * noise
        out[name] = jnp.asarray(drawn.astype(out[name].dtype))
    for name, factor in factors.items():
        out[name] = (out[name] * factor).astype(out[name].dtype)
    return out
```

```python
from contextlib import ExitStack

import concourse.bass as bass
from concourse import mybir

FIELDS, VOCAB, BATCH, D = 26, 12500, 2048, 64
BM1, BM2, TM1 = 128, 64, 256
P = 128
TILES = BATCH // P
SLOTS = FIELDS + 1
PAD = 32
QUAD = 32
GROUP = P // QUAD
HALF = P // 2
GROUPS = HALF // GROUP
ROUNDS = 4
RG = GROUPS // ROUNDS
SLABS = -(-SLOTS // GROUP)
COLS = SLABS * GROUP
BANK = 512
CHUNKS = [(0, 8), (8, 16), (16, 24), (24, 26)]
NPAIR = SLOTS * (SLOTS - 1) // 2


WP, BP, B1, B2, BT1, WT2, BT2 = 0, 1, 2, 3, 4, 6, 8
CONSTS = 9


def rec_kernel(nc, price, x_cat, table, consts, w1, w2, wt1_pairs, wt1_dense, out):
    fp32, i32, u32 = mybir.dt.float32, mybir.dt.int32, mybir.dt.uint32
    ALU, ACT = mybir.AluOpType, mybir.ActivationFunctionType

    with ExitStack() as ctx:
        def sb(name, shape, dt=fp32):
            return ctx.enter_context(nc.sbuf_tensor(name, shape, dt))

        def pb(name, shape):
            return ctx.enter_context(nc.psum_tensor(name, shape, fp32))

        def sem(name):
            return ctx.enter_context(nc.semaphore(name))

        raw_idx = sb("raw_idx", [P, TILES * FIELDS], i32)
        field_base = sb("field_base", [P, TILES * FIELDS], i32)
        wrap = sb("wrap", [P, TILES * FIELDS])
        wrapped = sb("wrapped", [P, TILES * FIELDS])
        clamped = sb("clamped", [P, TILES * FIELDS])
        row_idx = sb("row_idx", [P, (TILES + 1) * FIELDS])
        tile_idx = sb("tile_idx", [P, FIELDS], u32)
        gathered = sb("gathered", [P, FIELDS * D])
        feats = sb("feats", [P, HALF, PAD])
        gram = sb("gram", [P, SLABS * P])
        ident = sb("ident", [P, P])
        price_bc = sb("price_bc", [P, BATCH])
        dense = sb("dense", [D, P])
        hidden = sb("hidden", [BM1, P])
        dense_out = sb("dense_out", [BM2, P])
        top = sb("top", [P, 2 * P])
        scores = sb("scores", [1, BATCH])
        consts_sb = sb("consts_sb", [P, CONSTS])
        w1_sb, w2_sb = sb("w1_sb", [D, BM1]), sb("w2_sb", [BM1, BM2])
        wt1p_sb, wt1d_sb = sb("wt1p_sb", [P, SLABS * TM1]), sb("wt1d_sb", [BM2, TM1])

        def const(col, part=slice(0, P)):
            return consts_sb[part, col:col + 1]

        ps_gram = [pb(f"ps_gram{i}", [P, 2 * BANK]) for i in range(2)]
        ps_trans = [pb(f"ps_trans{i}", [P, BANK]) for i in range(2)]
        ps_mlp = pb("ps_mlp", [P, BANK])
        ps_score = pb("ps_score", [P, BANK])
        ps_top = [ps_mlp[:, 0:P], ps_mlp[:, P:2 * P]]
        ps_hidden = ps_mlp[:, 2 * P:3 * P]
        ps_dense_out = ps_mlp[0:BM2, 3 * P:4 * P]

        idx_loaded = sem("idx_loaded")
        base_made = sem("base_made")
        idx_step = sem("idx_step")
        small_loaded = sem("small_loaded")
        price_loaded = sem("price_loaded")
        pairs_loaded = sem("pairs_loaded")
        ident_zeroed = sem("ident_zeroed")
        ident_made = sem("ident_made")
        feats_zeroed = sem("feats_zeroed")
        tile_idx_set = [sem(f"tile_idx_set{c}") for c in range(len(CHUNKS))]
        chunk_gathered = [sem(f"chunk_gathered{c}") for c in range(len(CHUNKS))]
        chunk_transposed = [sem(f"chunk_transposed{c}") for c in range(len(CHUNKS))]
        trans_evacuated = sem("trans_evacuated")
        dense_made = sem("dense_made")
        dense_slot_set = sem("dense_slot_set")
        hidden_summed = sem("hidden_summed")
        hidden_made = sem("hidden_made")
        dense_out_summed = sem("dense_out_summed")
        dense_out_made = sem("dense_out_made")
        gram_done = sem("gram_done")
        gram_evac_dve = sem("gram_evac_dve")
        gram_evac_act = sem("gram_evac_act")
        top_summed = sem("top_summed")
        top_made = sem("top_made")
        score_summed = sem("score_summed")
        score_stored = sem("score_stored")
        out_written = sem("out_written")

        rows = table.rearrange("f v d -> (f v) d")
        NC = len(CHUNKS)

        gram_to = gram[:, :].rearrange("p (j h g s) -> p h g j s", j=SLABS, h=2, g=GROUPS, s=GROUP)
        gram_from = [ps[:, :].rearrange("p (h g s j c) -> p h g s j c", h=2, g=RG, s=GROUP, j=PAD // GROUP, c=GROUP)
                     for ps in ps_gram]

        def evacuate_gram(copy, r, quads):
            last = None
            for s in quads:
                for c in range(GROUP):
                    last = copy(gram_to[QUAD * c:QUAD * (c + 1), :, RG * r:RG * (r + 1), :, s],
                                gram_from[r % 2][QUAD * s:QUAD * (s + 1), :, :, s, 0:SLABS, c])
            return last

        block = ctx.enter_context(nc.Block())

        @block.sync
        def _(sp):
            sp.dma_start(raw_idx[:, :], x_cat).then_inc(idx_loaded, 16)
            sp.dma_start(price_bc[:, :], price.rearrange("(o b) -> o b", o=1).to_broadcast([P, BATCH])).then_inc(price_loaded, 16)
            sp.dma_start(wt1p_sb[:, :], wt1_pairs).then_inc(pairs_loaded, 16)
            sp.wait_ge(score_stored, TILES + 1)
            sp.dma_start(out.rearrange("(o b) -> o b", o=1), scores[:, :]).then_inc(out_written, 16)
            sp.wait_ge(out_written, 16)

        @block.gpsimd
        def _(pool):
            pool.iota(field_base[:, :], pattern=[[0, TILES], [VOCAB, FIELDS]], base=0, channel_multiplier=0)\
                .then_inc(base_made, 1)
            pool.memset(ident[:, :], 0.0).then_inc(ident_zeroed, 1)
            pool.wait_ge(ident_zeroed, 1)
            pool.affine_select(out=ident[:, :], in_=ident[:, :], compare_op=ALU.not_equal, fill=1.0,
                               base=0, pattern=[[-1, P]], channel_multiplier=1).then_inc(ident_made, 1)
            with pool.Fori(0, TILES) as t:
                for c, (f0, f1) in enumerate(CHUNKS):
                    pool.wait_ge(tile_idx_set[c], t + 1)
                    pool.nop(nofuse=True)
                    for f in range(f0, f1):
                        pool.indirect_dma_start(out=gathered[:, f * D:(f + 1) * D], out_offset=None, in_=rows,
                                                in_offset=bass.IndirectOffsetOnAxis(ap=tile_idx[:, f:f + 1], axis=0))\
                            .then_inc(chunk_gathered[c], 16)

        @block.scalar
        def _(act):
            act.dma_start(consts_sb[:, :], consts).then_inc(small_loaded, 16)
            act.dma_start(w1_sb[:, :], w1).then_inc(small_loaded, 16)
            act.dma_start(w2_sb[:, :], w2).then_inc(small_loaded, 16)
            act.dma_start(wt1d_sb[:, :], wt1_dense).then_inc(small_loaded, 16)
            act.wait_ge(small_loaded, 16 * 4)
            act.wait_ge(price_loaded, 16)
            act.wait_ge(feats_zeroed, 1)
            act.sem_inc(gram_evac_act, 2)
            act.sem_inc(score_stored, 1)

            def dense_features(dst, part, first, n, t):
                return nc.scalar.activation(dst, price_bc[part, bass.ds(t * P + first, n)], ACT.Identity,
                                            bias=const(BP, part), scale=const(WP, part))

            with act.Fori(0, TILES) as t:
                dense_features(dense[:, :], slice(0, D), 0, P, t).then_inc(dense_made, 1)
                dense_features(feats[0:D, :, 0], slice(0, D), 0, HALF, t).then_inc(dense_slot_set, 1)
                dense_features(feats[D:P, :, 0], slice(D, P), HALF, HALF, t).then_inc(dense_slot_set, 1)
                act.wait_ge(hidden_summed, t + 1)
                nc.scalar.activation(hidden[:, :], ps_hidden, ACT.Relu, bias=const(B1)).then_inc(hidden_made, 1)
                act.wait_ge(dense_out_summed, t + 1)
                nc.scalar.activation(dense_out[:, :], ps_dense_out, ACT.Relu, bias=const(B2, slice(0, BM2)))\
                    .then_inc(dense_out_made, 1)
                for c, (f0, f1) in enumerate(CHUNKS):
                    act.wait_ge(chunk_transposed[c], t + 1)
                    nc.scalar.copy(tile_idx[:, f0:f1], row_idx[:, bass.ds((t + 1) * FIELDS + f0, f1 - f0)])\
                        .then_inc(tile_idx_set[c], 1)
                for r in range(ROUNDS):
                    act.wait_ge(gram_done, ROUNDS * t + r + 1)
                    evacuate_gram(nc.scalar.copy, r, (2, 3)).then_inc(gram_evac_act, 1)
                act.wait_ge(top_summed, t + 1)
                nc.scalar.activation(top[:, 0:P], ps_top[0], ACT.Relu, bias=const(BT1)).then_inc(top_made, 1)
                nc.scalar.activation(top[:, P:2 * P], ps_top[1], ACT.Relu, bias=const(BT1 + 1)).then_inc(top_made, 1)
                act.wait_ge(score_summed, t + 1)
                nc.scalar.activation(scores[:, bass.ds(t * P, P)], ps_score[0:1, 0:P], ACT.Identity,
                                     bias=const(BT2, slice(0, 1))).then_inc(score_stored, 1)

        @block.vector
        def _(dve):
            dve.wait_ge(idx_loaded, 16)
            nc.vector.tensor_scalar(wrap[:, :], raw_idx[:, :], 0.0, float(VOCAB), ALU.is_lt, ALU.mult)\
                .then_inc(idx_step, 1)
            dve.wait_ge(idx_step, 1)
            nc.vector.tensor_tensor(wrapped[:, :], wrap[:, :], raw_idx[:, :], ALU.add).then_inc(idx_step, 1)
            dve.wait_ge(idx_step, 2)
            nc.vector.tensor_scalar(clamped[:, :], wrapped[:, :], 0.0, float(VOCAB - 1), ALU.max, ALU.min)\
                .then_inc(idx_step, 1)
            dve.wait_ge(idx_step, 3)
            dve.wait_ge(base_made, 1)
            nc.vector.tensor_tensor(row_idx[:, 0:TILES * FIELDS], clamped[:, :], field_base[:, :], ALU.add)\
                .then_inc(idx_step, 1)
            dve.wait_ge(idx_step, 4)
            for c, (f0, f1) in enumerate(CHUNKS):
                nc.vector.tensor_copy(tile_idx[:, f0:f1], row_idx[:, f0:f1]).then_inc(tile_idx_set[c], 1)
            nc.vector.memset(row_idx[:, TILES * FIELDS:], 0.0).then_inc(idx_step, 1)
            nc.vector.memset(feats[:, :, :], 0.0).then_inc(feats_zeroed, 1)
            dve.wait_ge(feats_zeroed, 1)
            dve.sem_inc(trans_evacuated, 2)
            dve.sem_inc(gram_evac_dve, 2)
            with dve.Fori(0, TILES) as t:
                for c, (f0, f1) in enumerate(CHUNKS):
                    dve.wait_ge(chunk_transposed[c], t + 1)
                    n = (f1 - f0) // 2
                    src = ps_trans[c % 2][:, 0:n * P].rearrange("p (k h b) -> p h b k", k=n, h=2)
                    for q in range(2):
                        for h in range(2):
                            last = nc.vector.tensor_copy(feats[D * h:D * (h + 1), :, 1 + f0 + q:f1 + q:2],
                                                         src[D * q:D * (q + 1), h, :, :])
                    last.then_inc(trans_evacuated, 1)
                for r in range(ROUNDS):
                    dve.wait_ge(gram_done, ROUNDS * t + r + 1)
                    evacuate_gram(nc.vector.tensor_copy, r, (0, 1)).then_inc(gram_evac_dve, 1)

        @block.tensor
        def _(pe):
            pe.wait_ge(ident_made, 1)
            pe.wait_ge(small_loaded, 16 * 4)
            pe.wait_ge(pairs_loaded, 16)

            def transpose_chunk(t, c):
                f0, f1 = CHUNKS[c]
                pe.wait_ge(chunk_gathered[c], 16 * (f1 - f0) * (t + 1))
                pe.wait_ge(trans_evacuated, NC * t + c + 1)
                for k in range((f1 - f0) // 2):
                    f = f0 + 2 * k
                    last = nc.tensor.transpose(ps_trans[c % 2][:, k * P:(k + 1) * P],
                                               gathered[:, f * D:(f + 2) * D], ident[:, :])
                last.then_inc(chunk_transposed[c], 1)

            with pe.Fori(0, TILES) as t:
                pe.wait_ge(dense_made, t + 1)
                nc.tensor.matmul(ps_hidden, w1_sb[:, :], dense[:, :], start=True, stop=True).then_inc(hidden_summed, 1)
                pe.wait_ge(hidden_made, t + 1)
                nc.tensor.matmul(ps_dense_out, w2_sb[:, :], hidden[:, :], start=True, stop=True)\
                    .then_inc(dense_out_summed, 1)
                for c in range(NC):
                    transpose_chunk(t, c)
                pe.wait_ge(trans_evacuated, NC * t + NC + 2)
                pe.wait_ge(dense_slot_set, 2 * t + 2)
                for r in range(ROUNDS):
                    pe.wait_ge(gram_evac_dve, ROUNDS * t + r + 1)
                    pe.wait_ge(gram_evac_act, ROUNDS * t + r + 1)
                    for g in range(RG):
                        for h in range(2):
                            at = (RG * r + g) * GROUP
                            f = feats[D * h:D * (h + 1), at:at + GROUP, :]
                            o = ps_gram[r % 2][:, h * BANK + g * P:h * BANK + (g + 1) * P]
                            last = nc.tensor.matmul(o.rearrange("p (s j) -> p s j", s=GROUP)[:, :, 0:COLS],
                                                    f.rearrange("p s j -> p (s j)"), f[:, :, 0:COLS],
                                                    start=True, stop=True)
                    last.then_inc(gram_done, 1)
                pe.wait_ge(dense_out_made, t + 1)
                pe.wait_ge(gram_evac_dve, ROUNDS * t + ROUNDS + 2)
                pe.wait_ge(gram_evac_act, ROUNDS * t + ROUNDS + 2)
                for m in range(2):
                    nc.tensor.matmul(ps_top[m], wt1d_sb[:, m * P:(m + 1) * P], dense_out[:, :], start=True, stop=False)
                    for j in range(SLABS):
                        last = nc.tensor.matmul(ps_top[m], wt1p_sb[:, j * TM1 + m * P:j * TM1 + (m + 1) * P],
                                                gram[:, j * P:(j + 1) * P], start=False, stop=(j == SLABS - 1))
                last.then_inc(top_summed, 1)
                pe.wait_ge(score_stored, t + 1)
                for m in range(2):
                    pe.wait_ge(top_made, 2 * t + 1 + m)
                    last = nc.tensor.matmul(ps_score[0:1, 0:P], const(WT2 + m), top[:, m * P:(m + 1) * P],
                                            start=(m == 0), stop=(m == 1))
                last.then_inc(score_summed, 1)


def pair_places():
    slot = [f + 1 for f in range(FIELDS)] + [0]
    places = []
    for a in range(SLOTS):
        for b in range(a + 1, SLOTS):
            i, j = sorted((slot[a], slot[b]))
            places.append((QUAD * (j % GROUP) + i, j // GROUP))
    return places


def kernel(**inputs):
    import numpy as _np
    import concourse.bacc as _bacc
    from concourse import mybir as _mybir
    from concourse.bass_utils import run_bass_kernel_spmd as _run

    x = {k: _np.asarray(v) for k, v in inputs.items()}
    wt1 = x["L0_rec_Wt1"]
    at = _np.array(pair_places())
    pairs = _np.zeros((P, SLABS, TM1), wt1.dtype)
    pairs[at[:, 0], at[:, 1]] = wt1[:NPAIR]
    consts = _np.zeros((P, CONSTS), wt1.dtype)
    for half in (0, D):
        consts[half:half + D, WP] = x["L0_rec_Wp"][0]
        consts[half:half + D, BP] = x["L0_rec_bp"]
    consts[:BM1, B1] = x["L0_rec_b1"]
    consts[:BM2, B2] = x["L0_rec_b2"]
    consts[:, BT1:BT1 + 2] = x["L0_rec_bt1"].reshape(2, P).T
    consts[:, WT2:WT2 + 2] = x["L0_rec_Wt2"].reshape(2, P).T
    consts[0, BT2] = x["L0_rec_bt2"][0]
    laid = {
        "price": x["r_price"],
        "x_cat": x["r_x_cat"].reshape(FIELDS, TILES, P).transpose(2, 1, 0).reshape(P, TILES * FIELDS),
        "table": x["L0_rec_emb_tables"],
        "consts": consts,
        "w1": x["L0_rec_W1"], "w2": x["L0_rec_W2"],
        "wt1_pairs": pairs.reshape(P, SLABS * TM1), "wt1_dense": wt1[NPAIR:],
    }
    nc = _bacc.Bacc("TRN2", target_bir_lowering=False, num_devices=1)
    arrays, args = {}, []
    for name, a in laid.items():
        a = _np.ascontiguousarray(a)
        arrays[f"in_{name}"] = a
        args.append(nc.dram_tensor(f"in_{name}", a.shape, _mybir.dt.from_np(a.dtype), kind="ExternalInput").ap())
    out = nc.dram_tensor("out_0", (BATCH,), _mybir.dt.float32, kind="ExternalOutput").ap()
    rec_kernel(nc, *args, out)
    r = _run(nc, [arrays], core_ids=[0])
    return r.results[0]["out_0"]
```

```python
from contextlib import ExitStack

import concourse.bass as bass
from concourse import mybir

FIELDS, VOCAB, BATCH, D = 26, 12500, 2048, 64
BM1, BM2, TM1 = 128, 64, 256
P = 128
TILES = BATCH // P
SLOTS = FIELDS + 1
PAD = 32
QUAD = 32
GROUP = P // QUAD
HALF = P // 2
GROUPS = HALF // GROUP
ROUNDS = 4
RG = GROUPS // ROUNDS
SLABS = -(-SLOTS // GROUP)
COLS = SLABS * GROUP
BANK = 512
CHUNKS = [(0, 8), (8, 16), (16, 24), (24, 26)]
NPAIR = SLOTS * (SLOTS - 1) // 2


WP, BP, B1, B2, BT1, WT2, BT2 = 0, 1, 2, 3, 4, 6, 8
CONSTS = 9


def rec_kernel(nc, price, x_cat, table, consts, w1, w2, wt1_pairs, wt1_dense, out):
    fp32, i32, u32 = mybir.dt.float32, mybir.dt.int32, mybir.dt.uint32
    ALU, ACT = mybir.AluOpType, mybir.ActivationFunctionType

    with ExitStack() as ctx:
        def sb(name, shape, dt=fp32):
            return ctx.enter_context(nc.sbuf_tensor(name, shape, dt))

        def pb(name, shape):
            return ctx.enter_context(nc.psum_tensor(name, shape, fp32))

        def sem(name):
            return ctx.enter_context(nc.semaphore(name))

        raw_idx = sb("raw_idx", [P, TILES * FIELDS], i32)
        field_base = sb("field_base", [P, TILES * FIELDS], i32)
        wrap = sb("wrap", [P, TILES * FIELDS])
        wrapped = sb("wrapped", [P, TILES * FIELDS])
        clamped = sb("clamped", [P, TILES * FIELDS])
        row_idx = sb("row_idx", [P, (TILES + 1) * FIELDS])
        tile_idx = sb("tile_idx", [P, FIELDS], u32)
        gathered = sb("gathered", [P, FIELDS * D])
        feats = sb("feats", [P, HALF, PAD])
        gram = sb("gram", [P, SLABS * P])
        ident = sb("ident", [P, P])
        price_bc = sb("price_bc", [P, BATCH])
        dense = sb("dense", [D, P])
        hidden = sb("hidden", [BM1, P])
        dense_out = sb("dense_out", [BM2, P])
        top = sb("top", [P, 2 * P])
        scores = sb("scores", [1, BATCH])
        consts_sb = sb("consts_sb", [P, CONSTS])
        w1_sb, w2_sb = sb("w1_sb", [D, BM1]), sb("w2_sb", [BM1, BM2])
        wt1p_sb, wt1d_sb = sb("wt1p_sb", [P, SLABS * TM1]), sb("wt1d_sb", [BM2, TM1])

        def const(col, part=slice(0, P)):
            return consts_sb[part, col:col + 1]

        ps_gram = [pb(f"ps_gram{i}", [P, 2 * BANK]) for i in range(2)]
        ps_trans = [pb(f"ps_trans{i}", [P, BANK]) for i in range(2)]
        ps_mlp = pb("ps_mlp", [P, BANK])
        ps_score = pb("ps_score", [P, BANK])
        ps_top = [ps_mlp[:, 0:P], ps_mlp[:, P:2 * P]]
        ps_hidden = ps_mlp[:, 2 * P:3 * P]
        ps_dense_out = ps_mlp[0:BM2, 3 * P:4 * P]

        idx_loaded = sem("idx_loaded")
        base_made = sem("base_made")
        idx_step = sem("idx_step")
        small_loaded = sem("small_loaded")
        price_loaded = sem("price_loaded")
        pairs_loaded = sem("pairs_loaded")
        ident_zeroed = sem("ident_zeroed")
        ident_made = sem("ident_made")
        feats_zeroed = sem("feats_zeroed")
        tile_idx_set = [sem(f"tile_idx_set{c}") for c in range(len(CHUNKS))]
        chunk_gathered = [sem(f"chunk_gathered{c}") for c in range(len(CHUNKS))]
        chunk_transposed = [sem(f"chunk_transposed{c}") for c in range(len(CHUNKS))]
        trans_evac_dve = sem("trans_evac_dve")
        trans_evac_act = sem("trans_evac_act")
        dense_made = sem("dense_made")
        dense_slot_set = sem("dense_slot_set")
        hidden_summed = sem("hidden_summed")
        hidden_made = sem("hidden_made")
        dense_out_summed = sem("dense_out_summed")
        dense_out_made = sem("dense_out_made")
        gram_done = sem("gram_done")
        gram_evac_dve = sem("gram_evac_dve")
        gram_evac_act = sem("gram_evac_act")
        top_summed = sem("top_summed")
        top_made = sem("top_made")
        score_summed = sem("score_summed")
        score_stored = sem("score_stored")
        out_written = sem("out_written")

        rows = table.rearrange("f v d -> (f v) d")
        NC = len(CHUNKS)

        gram_to = gram[:, :].rearrange("p (j h g s) -> p h g j s", j=SLABS, h=2, g=GROUPS, s=GROUP)
        gram_from = [ps[:, :].rearrange("p (h g s j c) -> p h g s j c", h=2, g=RG, s=GROUP, j=PAD // GROUP, c=GROUP)
                     for ps in ps_gram]

        def evacuate_gram(copy, r, quads):
            last = None
            for s in quads:
                for c in range(GROUP):
                    last = copy(gram_to[QUAD * c:QUAD * (c + 1), :, RG * r:RG * (r + 1), :, s],
                                gram_from[r % 2][QUAD * s:QUAD * (s + 1), :, :, s, 0:SLABS, c])
            return last

        def evacuate_chunk(copy, c, q):
            f0, f1 = CHUNKS[c]
            n = (f1 - f0) // 2
            src = ps_trans[c % 2][:, 0:n * P].rearrange("p (k h b) -> p h b k", k=n, h=2)
            for h in range(2):
                last = copy(feats[D * h:D * (h + 1), :, 1 + f0 + q:f1 + q:2], src[D * q:D * (q + 1), h, :, :])
            return last

        block = ctx.enter_context(nc.Block())

        @block.sync
        def _(sp):
            sp.dma_start(raw_idx[:, :], x_cat).then_inc(idx_loaded, 16)
            sp.dma_start(price_bc[:, :], price.rearrange("(o b) -> o b", o=1).to_broadcast([P, BATCH])).then_inc(price_loaded, 16)
            sp.dma_start(wt1p_sb[:, :], wt1_pairs).then_inc(pairs_loaded, 16)
            sp.wait_ge(score_stored, TILES + 1)
            sp.dma_start(out.rearrange("(o b) -> o b", o=1), scores[:, :]).then_inc(out_written, 16)
            sp.wait_ge(out_written, 16)

        @block.gpsimd
        def _(pool):
            pool.iota(field_base[:, :], pattern=[[0, TILES], [VOCAB, FIELDS]], base=0, channel_multiplier=0)\
                .then_inc(base_made, 1)
            pool.memset(ident[:, :], 0.0).then_inc(ident_zeroed, 1)
            pool.wait_ge(ident_zeroed, 1)
            pool.affine_select(out=ident[:, :], in_=ident[:, :], compare_op=ALU.not_equal, fill=1.0,
                               base=0, pattern=[[-1, P]], channel_multiplier=1).then_inc(ident_made, 1)
            with pool.Fori(0, TILES) as t:
                for c, (f0, f1) in enumerate(CHUNKS):
                    pool.wait_ge(tile_idx_set[c], t + 1)
                    pool.nop(nofuse=True)
                    for f in range(f0, f1):
                        pool.indirect_dma_start(out=gathered[:, f * D:(f + 1) * D], out_offset=None, in_=rows,
                                                in_offset=bass.IndirectOffsetOnAxis(ap=tile_idx[:, f:f + 1], axis=0))\
                            .then_inc(chunk_gathered[c], 16)

        @block.scalar
        def _(act):
            act.dma_start(consts_sb[:, :], consts).then_inc(small_loaded, 16)
            act.dma_start(w1_sb[:, :], w1).then_inc(small_loaded, 16)
            act.dma_start(w2_sb[:, :], w2).then_inc(small_loaded, 16)
            act.dma_start(wt1d_sb[:, :], wt1_dense).then_inc(small_loaded, 16)
            act.wait_ge(small_loaded, 16 * 4)
            act.wait_ge(price_loaded, 16)
            act.wait_ge(feats_zeroed, 1)
            act.sem_inc(trans_evac_act, 2)
            act.sem_inc(gram_evac_act, 2)
            act.sem_inc(score_stored, 1)

            def dense_features(dst, part, first, n, t):
                return nc.scalar.activation(dst, price_bc[part, bass.ds(t * P + first, n)], ACT.Identity,
                                            bias=const(BP, part), scale=const(WP, part))

            def odd_fields(c, t, next_indices=True):
                f0, f1 = CHUNKS[c]
                act.wait_ge(chunk_transposed[c], t + 1)
                if next_indices:
                    nc.scalar.copy(tile_idx[:, f0:f1], row_idx[:, bass.ds((t + 1) * FIELDS + f0, f1 - f0)])\
                        .then_inc(tile_idx_set[c], 1)
                evacuate_chunk(nc.scalar.copy, c, 1).then_inc(trans_evac_act, 1)

            def store_scores(t):
                act.wait_ge(score_summed, t + 1)
                nc.scalar.activation(scores[:, bass.ds(t * P, P)], ps_score[0:1, 0:P], ACT.Identity,
                                     bias=const(BT2, slice(0, 1))).then_inc(score_stored, 1)

            def tile(t, first, last):
                dense_features(dense[:, :], slice(0, D), 0, P, t).then_inc(dense_made, 1)
                dense_features(feats[0:D, :, 0], slice(0, D), 0, HALF, t).then_inc(dense_slot_set, 1)
                dense_features(feats[D:P, :, 0], slice(D, P), HALF, HALF, t).then_inc(dense_slot_set, 1)
                odd_fields(1, t, not last)
                act.wait_ge(hidden_summed, t + 1)
                nc.scalar.activation(hidden[:, :], ps_hidden, ACT.Relu, bias=const(B1)).then_inc(hidden_made, 1)
                odd_fields(2, t, not last)
                act.wait_ge(dense_out_summed, t + 1)
                nc.scalar.activation(dense_out[:, :], ps_dense_out, ACT.Relu, bias=const(B2, slice(0, BM2)))\
                    .then_inc(dense_out_made, 1)
                odd_fields(3, t, not last)
                if not first:
                    store_scores(t - 1)
                for r in range(ROUNDS):
                    act.wait_ge(gram_done, ROUNDS * t + r + 1)
                    evacuate_gram(nc.scalar.copy, r, (2, 3)).then_inc(gram_evac_act, 1)
                if not last:
                    odd_fields(0, t + 1)
                act.wait_ge(top_summed, t + 1)
                nc.scalar.activation(top[:, 0:P], ps_top[0], ACT.Relu, bias=const(BT1)).then_inc(top_made, 1)
                nc.scalar.activation(top[:, P:2 * P], ps_top[1], ACT.Relu, bias=const(BT1 + 1)).then_inc(top_made, 1)

            odd_fields(0, 0)
            tile(0, True, False)
            with act.Fori(1, TILES - 1) as t:
                tile(t, False, False)
            tile(TILES - 1, False, True)
            store_scores(TILES - 1)

        @block.vector
        def _(dve):
            dve.wait_ge(idx_loaded, 16)
            nc.vector.tensor_scalar(wrap[:, :], raw_idx[:, :], 0.0, float(VOCAB), ALU.is_lt, ALU.mult)\
                .then_inc(idx_step, 1)
            dve.wait_ge(idx_step, 1)
            nc.vector.tensor_tensor(wrapped[:, :], wrap[:, :], raw_idx[:, :], ALU.add).then_inc(idx_step, 1)
            dve.wait_ge(idx_step, 2)
            nc.vector.tensor_scalar(clamped[:, :], wrapped[:, :], 0.0, float(VOCAB - 1), ALU.max, ALU.min)\
                .then_inc(idx_step, 1)
            dve.wait_ge(idx_step, 3)
            dve.wait_ge(base_made, 1)
            nc.vector.tensor_tensor(row_idx[:, 0:TILES * FIELDS], clamped[:, :], field_base[:, :], ALU.add)\
                .then_inc(idx_step, 1)
            dve.wait_ge(idx_step, 4)
            for c, (f0, f1) in enumerate(CHUNKS):
                nc.vector.tensor_copy(tile_idx[:, f0:f1], row_idx[:, f0:f1]).then_inc(tile_idx_set[c], 1)
            nc.vector.memset(row_idx[:, TILES * FIELDS:], 0.0).then_inc(idx_step, 1)
            nc.vector.memset(feats[:, :, :], 0.0).then_inc(feats_zeroed, 1)
            dve.wait_ge(feats_zeroed, 1)
            dve.sem_inc(trans_evac_dve, 2)
            dve.sem_inc(gram_evac_dve, 2)

            def even_fields(c, t):
                dve.wait_ge(chunk_transposed[c], t + 1)
                evacuate_chunk(nc.vector.tensor_copy, c, 0).then_inc(trans_evac_dve, 1)

            def tile(t, last):
                for c in range(1, NC):
                    even_fields(c, t)
                for r in range(ROUNDS):
                    dve.wait_ge(gram_done, ROUNDS * t + r + 1)
                    evacuate_gram(nc.vector.tensor_copy, r, (0, 1)).then_inc(gram_evac_dve, 1)
                if not last:
                    even_fields(0, t + 1)

            even_fields(0, 0)
            with dve.Fori(0, TILES - 1) as t:
                tile(t, False)
            tile(TILES - 1, True)

        @block.tensor
        def _(pe):
            pe.wait_ge(ident_made, 1)
            pe.wait_ge(small_loaded, 16 * 4)
            pe.wait_ge(pairs_loaded, 16)

            def transpose_chunk(t, c):
                f0, f1 = CHUNKS[c]
                pe.wait_ge(chunk_gathered[c], 16 * (f1 - f0) * (t + 1))
                pe.wait_ge(trans_evac_dve, NC * t + c + 1)
                pe.wait_ge(trans_evac_act, NC * t + c + 1)
                for k in range((f1 - f0) // 2):
                    f = f0 + 2 * k
                    last = nc.tensor.transpose(ps_trans[c % 2][:, k * P:(k + 1) * P],
                                               gathered[:, f * D:(f + 2) * D], ident[:, :])
                last.then_inc(chunk_transposed[c], 1)

            def score(t):
                pe.wait_ge(score_stored, t + 1)
                for m in range(2):
                    pe.wait_ge(top_made, 2 * t + 1 + m)
                    last = nc.tensor.matmul(ps_score[0:1, 0:P], const(WT2 + m), top[:, m * P:(m + 1) * P],
                                            start=(m == 0), stop=(m == 1))
                last.then_inc(score_summed, 1)

            def tile(t, first, last_tile):
                transpose_chunk(t, 1)
                if not first:
                    score(t - 1)
                pe.wait_ge(dense_made, t + 1)
                nc.tensor.matmul(ps_hidden, w1_sb[:, :], dense[:, :], start=True, stop=True).then_inc(hidden_summed, 1)
                transpose_chunk(t, 2)
                pe.wait_ge(hidden_made, t + 1)
                nc.tensor.matmul(ps_dense_out, w2_sb[:, :], hidden[:, :], start=True, stop=True)\
                    .then_inc(dense_out_summed, 1)
                transpose_chunk(t, 3)
                pe.wait_ge(trans_evac_dve, NC * t + NC + 2)
                pe.wait_ge(trans_evac_act, NC * t + NC + 2)
                pe.wait_ge(dense_slot_set, 2 * t + 2)
                for r in range(ROUNDS):
                    pe.wait_ge(gram_evac_dve, ROUNDS * t + r + 1)
                    pe.wait_ge(gram_evac_act, ROUNDS * t + r + 1)
                    for g in range(RG):
                        for h in range(2):
                            at = (RG * r + g) * GROUP
                            f = feats[D * h:D * (h + 1), at:at + GROUP, :]
                            o = ps_gram[r % 2][:, h * BANK + g * P:h * BANK + (g + 1) * P]
                            last = nc.tensor.matmul(o.rearrange("p (s j) -> p s j", s=GROUP)[:, :, 0:COLS],
                                                    f.rearrange("p s j -> p (s j)"), f[:, :, 0:COLS],
                                                    start=True, stop=True)
                    last.then_inc(gram_done, 1)
                if not last_tile:
                    transpose_chunk(t + 1, 0)
                pe.wait_ge(dense_out_made, t + 1)
                pe.wait_ge(gram_evac_dve, ROUNDS * t + ROUNDS + 2)
                pe.wait_ge(gram_evac_act, ROUNDS * t + ROUNDS + 2)
                for m in range(2):
                    nc.tensor.matmul(ps_top[m], wt1d_sb[:, m * P:(m + 1) * P], dense_out[:, :], start=True, stop=False)
                    for j in range(SLABS):
                        last = nc.tensor.matmul(ps_top[m], wt1p_sb[:, j * TM1 + m * P:j * TM1 + (m + 1) * P],
                                                gram[:, j * P:(j + 1) * P], start=False, stop=(j == SLABS - 1))
                last.then_inc(top_summed, 1)

            transpose_chunk(0, 0)
            tile(0, True, False)
            with pe.Fori(1, TILES - 1) as t:
                tile(t, False, False)
            tile(TILES - 1, False, True)
            score(TILES - 1)


def pair_places():
    slot = [f + 1 for f in range(FIELDS)] + [0]
    places = []
    for a in range(SLOTS):
        for b in range(a + 1, SLOTS):
            i, j = sorted((slot[a], slot[b]))
            places.append((QUAD * (j % GROUP) + i, j // GROUP))
    return places


def kernel(**inputs):
    import numpy as _np
    import concourse.bacc as _bacc
    from concourse import mybir as _mybir
    from concourse.bass_utils import run_bass_kernel_spmd as _run

    x = {k: _np.asarray(v) for k, v in inputs.items()}
    wt1 = x["L0_rec_Wt1"]
    at = _np.array(pair_places())
    pairs = _np.zeros((P, SLABS, TM1), wt1.dtype)
    pairs[at[:, 0], at[:, 1]] = wt1[:NPAIR]
    consts = _np.zeros((P, CONSTS), wt1.dtype)
    for half in (0, D):
        consts[half:half + D, WP] = x["L0_rec_Wp"][0]
        consts[half:half + D, BP] = x["L0_rec_bp"]
    consts[:BM1, B1] = x["L0_rec_b1"]
    consts[:BM2, B2] = x["L0_rec_b2"]
    consts[:, BT1:BT1 + 2] = x["L0_rec_bt1"].reshape(2, P).T
    consts[:, WT2:WT2 + 2] = x["L0_rec_Wt2"].reshape(2, P).T
    consts[0, BT2] = x["L0_rec_bt2"][0]
    laid = {
        "price": x["r_price"],
        "x_cat": x["r_x_cat"].reshape(FIELDS, TILES, P).transpose(2, 1, 0).reshape(P, TILES * FIELDS),
        "table": x["L0_rec_emb_tables"],
        "consts": consts,
        "w1": x["L0_rec_W1"], "w2": x["L0_rec_W2"],
        "wt1_pairs": pairs.reshape(P, SLABS * TM1), "wt1_dense": wt1[NPAIR:],
    }
    nc = _bacc.Bacc("TRN2", target_bir_lowering=False, num_devices=1)
    arrays, args = {}, []
    for name, a in laid.items():
        a = _np.ascontiguousarray(a)
        arrays[f"in_{name}"] = a
        args.append(nc.dram_tensor(f"in_{name}", a.shape, _mybir.dt.from_np(a.dtype), kind="ExternalInput").ap())
    out = nc.dram_tensor("out_0", (BATCH,), _mybir.dt.float32, kind="ExternalOutput").ap()
    rec_kernel(nc, *args, out)
    r = _run(nc, [arrays], core_ids=[0])
    return r.results[0]["out_0"]
```

```python
from contextlib import ExitStack

import concourse.bass as bass
from concourse import mybir

FIELDS, VOCAB, BATCH, D = 26, 12500, 2048, 64
BM1, BM2, TM1 = 128, 64, 256
P = 128
TILES = BATCH // P
SLOTS = FIELDS + 1
PAD = 32
QUAD = 32
GROUP = P // QUAD
HALF = P // 2
UNITS = 2
UNIT = HALF // UNITS
GROUPS = HALF // GROUP
ROUNDS = 4
RG = GROUPS // ROUNDS
SLABS = -(-SLOTS // GROUP)
BANK = 512
CHUNKS = [(0, 8), (8, 16), (16, 24), (24, 26)]
WARM = {TILES - 2: (0, 12, 4, 1, 1), TILES - 1: (0, 7, 3, 1, 1)}
TO_GRAM, TO_TOP = 4, 5
NPAIR = SLOTS * (SLOTS - 1) // 2
WP, BP, B1, B2, BT1, WT2, BT2 = 0, 1, 2, 3, 4, 6, 8
CONSTS = 9


def rec_kernel(nc, price, x_cat, table, consts, w1, w2, wt1_pairs, wt1_dense, out):
    fp32, i32, u32 = mybir.dt.float32, mybir.dt.int32, mybir.dt.uint32
    ALU, ACT = mybir.AluOpType, mybir.ActivationFunctionType

    with ExitStack() as ctx:
        def sb(name, shape, dt=fp32):
            return ctx.enter_context(nc.sbuf_tensor(name, shape, dt))

        def pb(name, shape):
            return ctx.enter_context(nc.psum_tensor(name, shape, fp32))

        def sem(name):
            return ctx.enter_context(nc.semaphore(name))

        raw_idx = sb("raw_idx", [P, TILES * FIELDS], i32)
        field_base = sb("field_base", [P, FIELDS], i32)
        last_base = sb("last_base", [P, FIELDS], i32)
        wrap = sb("wrap", [P, TILES * FIELDS])
        wrapped = sb("wrapped", [P, TILES * FIELDS])
        clamped = sb("clamped", [P, TILES * FIELDS])
        row_idx = sb("row_idx", [P, (TILES + 1) * FIELDS])
        tile_idx = sb("tile_idx", [P, FIELDS], u32)
        gathered = sb("gathered", [P, FIELDS * D])
        feats = sb("feats", [P, HALF, PAD])
        gram = sb("gram", [P, SLABS * P])
        ident = sb("ident", [P, P])
        price_bc = sb("price_bc", [P, BATCH])
        dense = sb("dense", [D, P])
        hidden = sb("hidden", [BM1, P])
        dense_out = sb("dense_out", [BM2, P])
        top = sb("top", [P, 2 * P])
        scores = sb("scores", [1, BATCH])
        consts_sb = sb("consts_sb", [P, CONSTS])
        w1_sb, w2_sb = sb("w1_sb", [D, BM1]), sb("w2_sb", [BM1, BM2])
        wt1p_sb, wt1d_sb = sb("wt1p_sb", [P, SLABS * TM1]), sb("wt1d_sb", [BM2, TM1])

        def const(col, part=slice(0, P)):
            return consts_sb[part, col:col + 1]

        ps_gram = [pb(f"ps_gram{i}", [P, 2 * BANK]) for i in range(2)]
        ps_trans = [pb(f"ps_trans{i}", [P, BANK]) for i in range(2)]
        ps_mlp = [pb(f"ps_mlp{i}", [P, BANK]) for i in range(2)]
        ps_top = [ps_mlp[m][:, 0:P] for m in range(2)]
        ps_hidden = ps_mlp[0][:, P:2 * P]
        ps_dense_out = ps_mlp[0][0:BM2, 2 * P:3 * P]
        ps_score = ps_mlp[1][0:1, P:2 * P]

        first_idx_loaded = sem("first_idx_loaded")
        idx_loaded = sem("idx_loaded")
        base_made = sem("base_made")
        idx_step = sem("idx_step")
        rows_made = sem("rows_made")
        small_loaded = sem("small_loaded")
        price_loaded = sem("price_loaded")
        pairs_loaded = sem("pairs_loaded")
        ident_zeroed = sem("ident_zeroed")
        ident_made = sem("ident_made")
        feats_zeroed = sem("feats_zeroed")
        tile_idx_set = [sem(f"tile_idx_set{c}") for c in range(len(CHUNKS))]
        chunk_gathered = [sem(f"chunk_gathered{c}") for c in range(len(CHUNKS))]
        chunk_transposed = [sem(f"chunk_transposed{c}") for c in range(len(CHUNKS))]
        trans_evac_dve = sem("trans_evac_dve")
        trans_evac_act = sem("trans_evac_act")
        dense_made = sem("dense_made")
        dense_slot_set = sem("dense_slot_set")
        hidden_summed = sem("hidden_summed")
        hidden_made = sem("hidden_made")
        dense_out_summed = sem("dense_out_summed")
        dense_out_made = sem("dense_out_made")
        gram_done = sem("gram_done")
        gram_evac_dve = sem("gram_evac_dve")
        gram_evac_act = sem("gram_evac_act")
        top_summed = [sem(f"top_summed{m}") for m in range(2)]
        top_made = sem("top_made")
        score_summed = sem("score_summed")
        score_stored = sem("score_stored")
        out_written = sem("out_written")

        rows = table.rearrange("f v d -> (f v) d")
        NC = len(CHUNKS)

        gram_to = gram[:, :].rearrange("p (j h g s) -> p h g j s", j=SLABS, h=2, g=GROUPS, s=GROUP)
        gram_from = [ps[:, :].rearrange("p (h g s j c) -> p h g s j c", h=2, g=RG, s=GROUP, j=PAD // GROUP, c=GROUP)
                     for ps in ps_gram]

        def evacuate_gram(copy, r, quads):
            for s in quads:
                for c in range(GROUP):
                    last = copy(gram_to[QUAD * c:QUAD * (c + 1), :, RG * r:RG * (r + 1), :, s],
                                gram_from[r % 2][QUAD * s:QUAD * (s + 1), :, :, s, 0:SLABS, c])
            return last

        def evacuate_chunk(copy, c, q):
            f0, f1 = CHUNKS[c]
            n = (f1 - f0) // 2
            src = ps_trans[c % 2][:, 0:n * P].rearrange("p (k h b) -> p h b k", k=n, h=2)
            for h in range(2):
                last = copy(feats[D * h:D * (h + 1), :, 1 + f0 + q:f1 + q:2], src[D * q:D * (q + 1), h, :, :])
            return last

        def evacuate_unit_chunk(copy, c, kk):
            f0, f1 = CHUNKS[c]
            src = ps_trans[c % 2][:, :].rearrange("p (m q h b) -> p m q h b", m=BANK // P, q=2, h=2)
            for u in range(UNITS):
                slots = [s for s in range(f0 + kk, f1, 2) if s // (FIELDS // 2) == u]
                if not slots:
                    continue
                m0, n, f = (slots[0] - f0) // 2, len(slots), 1 + 2 * (slots[0] % (FIELDS // 2))
                for h in range(2):
                    dst = feats[D * h:D * (h + 1), UNIT * u:UNIT * (u + 1), f:f + 4 * n]
                    dst = dst.rearrange("p b (m r) -> p m r b", r=4)[:, :, 0:2, :]
                    last = copy(dst, src[D * kk:D * (kk + 1), m0:m0 + n, :, h, :])
            return last

        block = ctx.enter_context(nc.Block())

        @block.sync
        def _(sp):
            sp.dma_start(raw_idx[:, 0:FIELDS], x_cat[:, 0:FIELDS]).then_inc(first_idx_loaded, 16)
            sp.dma_start(raw_idx[:, FIELDS:], x_cat[:, FIELDS:]).then_inc(idx_loaded, 16)
            sp.dma_start(price_bc[:, :], price.rearrange("(o b) -> o b", o=1).to_broadcast([P, BATCH])).then_inc(price_loaded, 16)
            sp.dma_start(wt1p_sb[:, :], wt1_pairs).then_inc(pairs_loaded, 16)
            sp.wait_ge(score_stored, TILES + 1)
            sp.dma_start(out.rearrange("(o b) -> o b", o=1), scores[:, :]).then_inc(out_written, 16)
            sp.wait_ge(out_written, 16)

        @block.gpsimd
        def _(pool):
            pool.iota(field_base[:, :], pattern=[[VOCAB, FIELDS]], base=0, channel_multiplier=0).then_inc(base_made, 1)
            for q in range(2):
                pool.wait_ge(base_made, q + 1)
                pool.iota(last_base[HALF * q:HALF * (q + 1), :], pattern=[[0, UNITS], [2 * VOCAB, FIELDS // 2]],
                          base=q * VOCAB, channel_multiplier=0).then_inc(base_made, 1)
            pool.wait_ge(base_made, 3)
            pool.memset(ident[:, :], 0.0).then_inc(ident_zeroed, 1)
            pool.wait_ge(ident_zeroed, 1)
            pool.affine_select(out=ident[:, :], in_=ident[:, :], compare_op=ALU.not_equal, fill=1.0,
                               base=0, pattern=[[-1, P]], channel_multiplier=1).then_inc(ident_made, 1)
            with pool.Fori(0, TILES) as t:
                for c, (f0, f1) in enumerate(CHUNKS):
                    pool.wait_ge(tile_idx_set[c], t + 1)
                    pool.nop(nofuse=True)
                    for f in range(f0, f1):
                        pool.indirect_dma_start(out=gathered[:, f * D:(f + 1) * D], out_offset=None, in_=rows,
                                                in_offset=bass.IndirectOffsetOnAxis(ap=tile_idx[:, f:f + 1], axis=0))\
                            .then_inc(chunk_gathered[c], 16)

        @block.scalar
        def _(act):
            act.dma_start(consts_sb[:, :], consts).then_inc(small_loaded, 16)
            act.dma_start(w1_sb[:, :], w1).then_inc(small_loaded, 16)
            act.dma_start(w2_sb[:, :], w2).then_inc(small_loaded, 16)
            act.dma_start(wt1d_sb[:, :], wt1_dense).then_inc(small_loaded, 16)
            act.wait_ge(small_loaded, 16 * 4)
            act.wait_ge(price_loaded, 16)
            act.wait_ge(feats_zeroed, 1)
            act.wait_ge(rows_made, 3)
            act.sem_inc(trans_evac_act, 2)
            act.sem_inc(gram_evac_act, 2)
            act.sem_inc(score_stored, 1)

            def dense_features(dst, part, first, n, t):
                return nc.scalar.activation(dst, price_bc[part, bass.ds(t * P + first, n)], ACT.Identity,
                                            bias=const(BP, part), scale=const(WP, part))

            def odd_fields(c, t, next_indices=True, evacuate=evacuate_chunk):
                f0, f1 = CHUNKS[c]
                act.wait_ge(chunk_transposed[c], t + 1)
                if next_indices:
                    nc.scalar.copy(tile_idx[:, f0:f1], row_idx[:, bass.ds((t + 1) * FIELDS + f0, f1 - f0)])\
                        .then_inc(tile_idx_set[c], 1)
                evacuate(nc.scalar.copy, c, 1).then_inc(trans_evac_act, 1)

            def gram_round(r, t):
                act.wait_ge(gram_done, ROUNDS * t + r + 1)
                evacuate_gram(nc.scalar.copy, r, (2, 3)).then_inc(gram_evac_act, 1)

            def dense_parts(t):
                dense_features(dense[:, :], slice(0, D), 0, P, t).then_inc(dense_made, 1)
                dense_features(feats[0:D, :, 0], slice(0, D), 0, HALF, t).then_inc(dense_slot_set, 1)
                dense_features(feats[D:P, :, 0], slice(D, P), HALF, HALF, t).then_inc(dense_slot_set, 1)

            def hidden_relu(t):
                act.wait_ge(hidden_summed, t + 1)
                nc.scalar.activation(hidden[:, :], ps_hidden, ACT.Relu, bias=const(B1)).then_inc(hidden_made, 1)

            def dense_out_relu(t):
                act.wait_ge(dense_out_summed, t + 1)
                nc.scalar.activation(dense_out[:, :], ps_dense_out, ACT.Relu, bias=const(B2, slice(0, BM2)))\
                    .then_inc(dense_out_made, 1)

            def top_relu(t):
                act.wait_ge(top_summed[0], t + 1)
                nc.scalar.activation(top[:, 0:P], ps_top[0], ACT.Relu, bias=const(BT1)).then_inc(top_made, 1)

            def store_scores(t):
                act.wait_ge(score_summed, t + 1)
                nc.scalar.activation(scores[:, bass.ds(t * P, P)], ps_score, ACT.Identity,
                                     bias=const(BT2, slice(0, 1))).then_inc(score_stored, 1)

            def tile(t, first=False, next_evacuate=evacuate_chunk):
                dense_parts(t)
                odd_fields(1, t)
                hidden_relu(t)
                odd_fields(2, t)
                dense_out_relu(t)
                odd_fields(3, t)
                if not first:
                    store_scores(t - 1)
                for r in range(ROUNDS):
                    gram_round(r, t)
                odd_fields(0, t + 1, evacuate=next_evacuate)
                top_relu(t)

            odd_fields(0, 0)
            tile(0, first=True)
            with act.Fori(1, TILES - 2) as t:
                tile(t)
            tile(TILES - 2, next_evacuate=evacuate_unit_chunk)
            t = TILES - 1
            dense_parts(t)
            odd_fields(1, t, False, evacuate_unit_chunk)
            hidden_relu(t)
            dense_out_relu(t)
            store_scores(t - 1)
            for r in range(ROUNDS // 2):
                gram_round(r, t)
            odd_fields(2, t, False, evacuate_unit_chunk)
            odd_fields(3, t, False, evacuate_unit_chunk)
            for r in range(ROUNDS // 2, ROUNDS):
                gram_round(r, t)
            top_relu(t)
            store_scores(t)

        @block.vector
        def _(dve):
            steps = [0]

            def step(instruction):
                instruction.then_inc(idx_step, 1)
                steps[0] += 1
                dve.wait_ge(idx_step, steps[0])

            def clamp(a, b):
                step(nc.vector.tensor_scalar(wrap[:, a:b], raw_idx[:, a:b], 0.0, float(VOCAB), ALU.is_lt, ALU.mult))
                step(nc.vector.tensor_tensor(wrapped[:, a:b], wrap[:, a:b], raw_idx[:, a:b], ALU.add))
                step(nc.vector.tensor_scalar(clamped[:, a:b], wrapped[:, a:b], 0.0, float(VOCAB - 1), ALU.max, ALU.min))

            dve.wait_ge(first_idx_loaded, 16)
            clamp(0, FIELDS)
            dve.wait_ge(base_made, 3)
            for c, (f0, f1) in enumerate(CHUNKS):
                nc.vector.tensor_tensor(tile_idx[:, f0:f1], clamped[:, f0:f1], field_base[:, f0:f1], ALU.add)\
                    .then_inc(tile_idx_set[c], 1)
            dve.wait_ge(idx_loaded, 16)
            clamp(FIELDS, TILES * FIELDS)
            a, b = FIELDS, (TILES - 1) * FIELDS
            nc.vector.tensor_tensor(row_idx[:, a:b].rearrange("p (t f) -> p t f", f=FIELDS),
                                    clamped[:, a:b].rearrange("p (t f) -> p t f", f=FIELDS),
                                    field_base[:, :].rearrange("p (o f) -> p o f", o=1)
                                    .to_broadcast([P, TILES - 2, FIELDS]), ALU.add).then_inc(rows_made, 1)
            nc.vector.tensor_tensor(row_idx[:, b:b + FIELDS], clamped[:, b:b + FIELDS], last_base[:, :], ALU.add)\
                .then_inc(rows_made, 1)
            nc.vector.memset(row_idx[:, TILES * FIELDS:], 0.0).then_inc(rows_made, 1)
            nc.vector.memset(feats[:, :, :], 0.0).then_inc(feats_zeroed, 1)
            dve.wait_ge(feats_zeroed, 1)
            dve.wait_ge(small_loaded, 16 * 4)
            dve.sem_inc(trans_evac_dve, 2)
            dve.sem_inc(gram_evac_dve, 2)

            def even_fields(c, t, evacuate=evacuate_chunk):
                dve.wait_ge(chunk_transposed[c], t + 1)
                evacuate(nc.vector.tensor_copy, c, 0).then_inc(trans_evac_dve, 1)

            def gram_round(r, t):
                dve.wait_ge(gram_done, ROUNDS * t + r + 1)
                evacuate_gram(nc.vector.tensor_copy, r, (0, 1)).then_inc(gram_evac_dve, 1)

            def top_relu(t):
                dve.wait_ge(top_summed[1], t + 1)
                nc.vector.tensor_scalar(top[:, P:2 * P], ps_top[1], const(BT1 + 1), 0.0, ALU.add, ALU.max)\
                    .then_inc(top_made, 1)

            def tile(t, next_evacuate=evacuate_chunk):
                for c in range(1, NC):
                    even_fields(c, t)
                for r in range(ROUNDS):
                    gram_round(r, t)
                even_fields(0, t + 1, next_evacuate)
                top_relu(t)

            even_fields(0, 0)
            with dve.Fori(0, TILES - 2) as t:
                tile(t)
            tile(TILES - 2, evacuate_unit_chunk)
            t = TILES - 1
            even_fields(1, t, evacuate_unit_chunk)
            for r in range(ROUNDS // 2):
                gram_round(r, t)
            even_fields(2, t, evacuate_unit_chunk)
            even_fields(3, t, evacuate_unit_chunk)
            for r in range(ROUNDS // 2, ROUNDS):
                gram_round(r, t)
            top_relu(t)

        @block.tensor
        def _(pe):
            pe.wait_ge(ident_made, 1)
            pe.wait_ge(small_loaded, 16 * 4)
            pe.wait_ge(pairs_loaded, 16)

            def keep_warm(t, place, bank):
                if isinstance(t, int) and t in WARM and place > 0:
                    for _ in range(WARM[t][place - 1]):
                        nc.tensor.matmul(ps_trans[bank][:, 0:TM1], ident[:, :], wt1p_sb[:, 0:TM1], start=True, stop=True)

            def transpose_chunk(t, c):
                f0, f1 = CHUNKS[c]
                pe.wait_ge(trans_evac_dve, NC * t + c + 1)
                pe.wait_ge(trans_evac_act, NC * t + c + 1)
                keep_warm(t, c, c % 2)
                pe.wait_ge(chunk_gathered[c], 16 * (f1 - f0) * (t + 1))
                for k in range((f1 - f0) // 2):
                    f = f0 + 2 * k
                    last = nc.tensor.transpose(ps_trans[c % 2][:, k * P:(k + 1) * P],
                                               gathered[:, f * D:(f + 2) * D], ident[:, :])
                last.then_inc(chunk_transposed[c], 1)

            def hidden_layer(t):
                pe.wait_ge(dense_made, t + 1)
                nc.tensor.matmul(ps_hidden, w1_sb[:, :], dense[:, :], start=True, stop=True).then_inc(hidden_summed, 1)

            def dense_out_layer(t):
                pe.wait_ge(hidden_made, t + 1)
                nc.tensor.matmul(ps_dense_out, w2_sb[:, :], hidden[:, :], start=True, stop=True)\
                    .then_inc(dense_out_summed, 1)

            def gram_rounds(t, rounds, chunks):
                if chunks == NC and isinstance(t, int):
                    pe.wait_ge(trans_evac_dve, NC * t + NC + 1)
                    pe.wait_ge(trans_evac_act, NC * t + NC + 1)
                    keep_warm(t, TO_GRAM, 0)
                pe.wait_ge(trans_evac_dve, NC * t + chunks + 2)
                pe.wait_ge(trans_evac_act, NC * t + chunks + 2)
                pe.wait_ge(dense_slot_set, 2 * t + 2)
                for r in rounds:
                    pe.wait_ge(gram_evac_dve, ROUNDS * t + r + 1)
                    pe.wait_ge(gram_evac_act, ROUNDS * t + r + 1)
                    for g in range(RG):
                        for h in range(2):
                            at = (RG * r + g) * GROUP
                            group = feats[D * h:D * (h + 1), at:at + GROUP, :].rearrange("p s j -> p (s j)")
                            last = nc.tensor.matmul(ps_gram[r % 2][:, h * BANK + g * P:h * BANK + (g + 1) * P],
                                                    group, group, start=True, stop=True)
                    last.then_inc(gram_done, 1)

            def top_layer(t):
                for m in range(2):
                    if m == 0:
                        pe.wait_ge(dense_out_made, t + 1)
                    else:
                        pe.wait_ge(score_stored, t + 1)
                    nc.tensor.matmul(ps_top[m], wt1d_sb[:, m * P:(m + 1) * P], dense_out[:, :], start=True, stop=False)
                    if m == 0:
                        keep_warm(t, TO_TOP, 1)
                        pe.wait_ge(gram_evac_dve, ROUNDS * t + ROUNDS + 2)
                        pe.wait_ge(gram_evac_act, ROUNDS * t + ROUNDS + 2)
                    for j in range(SLABS):
                        last = nc.tensor.matmul(ps_top[m], wt1p_sb[:, j * TM1 + m * P:j * TM1 + (m + 1) * P],
                                                gram[:, j * P:(j + 1) * P], start=False, stop=(j == SLABS - 1))
                    last.then_inc(top_summed[m], 1)

            def score(t):
                pe.wait_ge(top_made, 2 * t + 2)
                for m in range(2):
                    last = nc.tensor.matmul(ps_score, const(WT2 + m), top[:, m * P:(m + 1) * P],
                                            start=(m == 0), stop=(m == 1))
                last.then_inc(score_summed, 1)

            def tile(t, first=False):
                transpose_chunk(t, 1)
                if not first:
                    score(t - 1)
                hidden_layer(t)
                transpose_chunk(t, 2)
                dense_out_layer(t)
                transpose_chunk(t, 3)
                gram_rounds(t, range(ROUNDS), NC)
                transpose_chunk(t + 1, 0)
                top_layer(t)

            transpose_chunk(0, 0)
            tile(0, first=True)
            with pe.Fori(1, TILES - 2) as t:
                tile(t)
            tile(TILES - 2)
            t = TILES - 1
            transpose_chunk(t, 1)
            score(t - 1)
            hidden_layer(t)
            dense_out_layer(t)
            gram_rounds(t, range(ROUNDS // 2), 2)
            transpose_chunk(t, 2)
            transpose_chunk(t, 3)
            gram_rounds(t, range(ROUNDS // 2, ROUNDS), NC)
            top_layer(t)
            score(t)


def pair_places():
    slot = [f + 1 for f in range(FIELDS)] + [0]
    places = []
    for a in range(SLOTS):
        for b in range(a + 1, SLOTS):
            i, j = sorted((slot[a], slot[b]))
            places.append((QUAD * (j % GROUP) + i, j // GROUP))
    return places


def kernel(**inputs):
    import numpy as _np
    import concourse.bacc as _bacc
    from concourse import mybir as _mybir
    from concourse.bass_utils import run_bass_kernel_spmd as _run

    x = {k: _np.asarray(v) for k, v in inputs.items()}
    wt1 = x["L0_rec_Wt1"]
    at = _np.array(pair_places())
    pairs = _np.zeros((P, SLABS, TM1), wt1.dtype)
    pairs[at[:, 0], at[:, 1]] = wt1[:NPAIR]
    consts = _np.zeros((P, CONSTS), wt1.dtype)
    for half in (0, D):
        consts[half:half + D, WP] = x["L0_rec_Wp"][0]
        consts[half:half + D, BP] = x["L0_rec_bp"]
    consts[:BM1, B1] = x["L0_rec_b1"]
    consts[:BM2, B2] = x["L0_rec_b2"]
    consts[:, BT1:BT1 + 2] = x["L0_rec_bt1"].reshape(2, P).T
    consts[:, WT2:WT2 + 2] = x["L0_rec_Wt2"].reshape(2, P).T
    consts[0, BT2] = x["L0_rec_bt2"][0]
    cat = x["r_x_cat"].reshape(FIELDS, TILES, P)
    idx = cat.transpose(2, 1, 0).copy()
    idx[:, -1] = cat[:, -1].reshape(FIELDS // 2, 2, 2, UNITS, UNIT).transpose(1, 2, 4, 3, 0).reshape(P, FIELDS)
    idx = idx.reshape(P, TILES * FIELDS)
    laid = {
        "price": x["r_price"],
        "x_cat": idx,
        "table": x["L0_rec_emb_tables"],
        "consts": consts,
        "w1": x["L0_rec_W1"], "w2": x["L0_rec_W2"],
        "wt1_pairs": pairs.reshape(P, SLABS * TM1), "wt1_dense": wt1[NPAIR:],
    }
    nc = _bacc.Bacc("TRN2", target_bir_lowering=False, num_devices=1)
    arrays, args = {}, []
    for name, a in laid.items():
        a = _np.ascontiguousarray(a)
        arrays[f"in_{name}"] = a
        args.append(nc.dram_tensor(f"in_{name}", a.shape, _mybir.dt.from_np(a.dtype), kind="ExternalInput").ap())
    out = nc.dram_tensor("out_0", (BATCH,), _mybir.dt.float32, kind="ExternalOutput").ap()
    rec_kernel(nc, *args, out)
    r = _run(nc, [arrays], core_ids=[0])
    return r.results[0]["out_0"]
```
